# Optimizing a Trainium2 kernel written in Bass

```python
import numpy as np
import jax
import jax.numpy as jnp

def _softmax(x, axis=-1):
    return jax.nn.softmax(x, axis=axis)

def _gelu(x):
    return jax.nn.gelu(x, approximate=True)

def _silu(x):
    return jax.nn.silu(x)

def _sigmoid(x):
    return jax.nn.sigmoid(x)

def _layernorm(x, axis=-1, eps=1e-05):
    m = jnp.mean(x, axis=axis, keepdims=True)
    v = jnp.var(x, axis=axis, keepdims=True)
    return (x - m) / jnp.sqrt(v + eps)

def _scatter_add(tgt, idx, src, axis=0):
    return tgt.at[idx].add(src)

def _segment_sum(src, seg, n):
    return jax.ops.segment_sum(src, seg, n)
kernel_name = 'mk_cond_resid_d1_seqx_r4_8e56b4'

def setup_inputs(seed: int=0):
    np.random.seed(seed)
    _w = jnp.asarray

    def _rec_inputs():
        import jax
        import jax.numpy as jnp
        _rk = jax.random.key(seed)
        x = -0.0003929 + 0.9999 * jax.random.normal(jax.random.fold_in(_rk, 1), (4, 512, 256), jnp.float32)
        _lenS = 512 - jax.random.randint(jax.random.fold_in(_rk, 7), (4,), 0, max(1, 512 // 4) + 1, jnp.int32)
        _lenS2 = 512 - jax.random.randint(jax.random.fold_in(_rk, 8), (4,), 0, max(1, 512 // 4) + 1, jnp.int32)
        itok_BxS_2_50255 = jax.random.randint(jax.random.fold_in(_rk, 11), (4, 512), 2, 12564, jnp.int32)
        cond_1024 = -0.00920427 + 1.00102 * jax.random.normal(jax.random.fold_in(_rk, 12), (4, 256), jnp.float32)
        return (x, itok_BxS_2_50255, cond_1024)
    x, itok_BxS_2_50255, cond_1024 = _rec_inputs()

    def _L0_cond_setup():
        import jax, jax.numpy as jnp
        import numpy as np
        HASH_PRIME = 5099
        MIN_CAPACITY = 4
        key = jax.random.key(seed)
        ks = jax.random.split(key, 8)
        B, T, D, F, E = (8, 512, 256, 512, 16)
        return {'x': jax.random.normal(ks[0], (B, T, D), dtype=jnp.float32), 'token_ids': jax.random.randint(ks[1], (B, T), 0, 50257, dtype=jnp.int32), 'shift_state': jax.random.normal(ks[2], (B, D), dtype=jnp.float32), 'time_maa_k': jax.random.uniform(ks[3], (D,), dtype=jnp.float32), 'time_maa_r': jax.random.uniform(ks[4], (D,), dtype=jnp.float32), 'w_recept': jax.random.normal(ks[5], (D, D), dtype=jnp.float32) * 0.02, 'w_key': jax.random.normal(ks[6], (E, D, F), dtype=jnp.float32) * 0.02, 'w_value': jax.random.normal(ks[7], (E, F, D), dtype=jnp.float32) * 0.02}
    _L0_cond_all = _L0_cond_setup()
    _L0_cond_in = {k: v for k, v in _L0_cond_all.items() if k in ('time_maa_k', 'time_maa_r', 'w_recept', 'w_key', 'w_value')}
    del _L0_cond_all
    return {'x': x, 'itok_BxS_2_50255': itok_BxS_2_50255, 'cond_1024': cond_1024, 'L0_cond_time_maa_k': _L0_cond_in['time_maa_k'], 'L0_cond_time_maa_r': _L0_cond_in['time_maa_r'], 'L0_cond_w_recept': _L0_cond_in['w_recept'], 'L0_cond_w_key': _L0_cond_in['w_key'], 'L0_cond_w_value': _L0_cond_in['w_value']}

def reference(x, itok_BxS_2_50255, cond_1024, L0_cond_time_maa_k, L0_cond_time_maa_r, L0_cond_w_recept, L0_cond_w_key, L0_cond_w_value):
    import jax
    import jax.numpy as jnp

    def _L0_cond_ref(x, token_ids, shift_state, time_maa_k, time_maa_r, w_recept, w_key, w_value):
        import jax, jax.numpy as jnp
        import numpy as np
        HASH_PRIME = 5099
        MIN_CAPACITY = 4
        B, T, D = x.shape
        E = w_key.shape[0]
        N = B * T
        C = max(MIN_CAPACITY, N // E)
        xprev = jnp.concatenate([shift_state[:, None, :], x[:, :-1]], axis=1)
        dxprev = xprev - x
        xk = x + dxprev * time_maa_k
        xr = x + dxprev * time_maa_r
        e_idx = token_ids.reshape(N).astype(jnp.int32) * HASH_PRIME % E
        onehot = (e_idx[:, None] == jnp.arange(E, dtype=jnp.int32)[None, :]).astype(jnp.int32)
        pos = jnp.take_along_axis(jnp.cumsum(onehot, axis=0), e_idx[:, None], axis=1)[:, 0] - 1
        keep = pos < C
        slot = jnp.where(keep, e_idx * C + pos, E * C)
        xk_flat = xk.reshape(N, D)
        buf = jnp.zeros((E * C + 1, D), dtype=x.dtype).at[slot].set(xk_flat)
        expert_in = buf[:E * C].reshape(E, C, D)
        h = jnp.square(jax.nn.relu(jnp.einsum('ecd,edf->ecf', expert_in, w_key)))
        expert_out = jnp.einsum('ecf,efd->ecd', h, w_value)
        out_pad = jnp.concatenate([expert_out.reshape(E * C, D), jnp.zeros((1, D), dtype=x.dtype)], axis=0)
        y = out_pad[slot].reshape(B, T, D)
        r = jax.nn.sigmoid(jnp.einsum('btd,ed->bte', xr, w_recept))
        return r * y
    x = x + _L0_cond_ref(x, itok_BxS_2_50255, cond_1024, L0_cond_time_maa_k, L0_cond_time_maa_r, L0_cond_w_recept, L0_cond_w_key, L0_cond_w_value)
    return x

_drawn_inputs = setup_inputs


def setup_inputs(seed=0):
    import zlib

    import numpy as np

    out = dict(_drawn_inputs(seed))
    spreads = {}
    factors = {'cond_1024': 8.0,
     'L0_cond_time_maa_k': 5.961,
     'L0_cond_time_maa_r': 8.0,
     'L0_cond_w_recept': 8.0,
     'L0_cond_w_key': 3.406,
     'L0_cond_w_value': 3.107}
    for name, (base, spread) in spreads.items():
        noise = np.random.default_rng([zlib.crc32(name.encode()), seed]).standard_normal(out[name].shape)
        drawn = base * np.exp(spread * noise) if base else spread * noise
        out[name] = jnp.asarray(drawn.astype(out[name].dtype))
    for name, factor in factors.items():
        out[name] = (out[name] * factor).astype(out[name].dtype)
    return out
```

```python
from contextlib import ExitStack

import concourse.bass as bass
from concourse import mybir

P = 128
HASH_PRIME = 5099

ALU = mybir.AluOpType
ACT = mybir.ActivationFunctionType
AX_X = mybir.AxisListType.X
F32 = mybir.dt.float32
BF16 = mybir.dt.bfloat16
I32 = mybir.dt.int32
U32 = mybir.dt.uint32

SLOTS = 4


def build(nc, x, pairs, ids, consts, weights, out):
    B, T, D = x.shape
    N = B * T
    E = weights.shape[0]
    DK = D // P
    F = weights.shape[2] // (2 * DK)
    FK = F // P
    C = N // E
    K = N // P
    assert C == P and DK == 2 and E == 16 and FK == 4 and K == 16
    HALF = FK // 2 * C
    NO_ROW = 2 * N
    ROUNDS = E // SLOTS

    out_rows = out.rearrange("b t d -> (b t) d")

    with ExitStack() as ctx:
        def sb(name, shape, dt=F32):
            return ctx.enter_context(nc.sbuf_tensor(name, shape, dt))

        def psum(name, cols):
            return ctx.enter_context(nc.psum_tensor(name, [P, cols], F32))

        def sem(name):
            return ctx.enter_context(nc.semaphore(name))

        tok = sb("tok", [P, K], I32)
        tok_low = sb("tok_low", [P, K], I32)
        etab3 = sb("etab3", [P, E, K], I32)
        etab = sb("etab", [P, E, K], I32)
        not_first = sb("not_first", [P, E, K], BF16)
        k_plus1 = sb("k_plus1", [P, E, K], BF16)
        p_times_k = sb("p_times_k", [P, 1])
        slot_no = sb("slot_no", [P, C], BF16)
        earlier = sb("earlier", [P, P], BF16)
        ident = sb("ident", [P, P])
        onehot = sb("onehot", [P, E, K], BF16)
        running = sb("running", [P, E, K])
        counts = sb("counts", [P, E], BF16)
        ranked = sb("ranked", [P, E, K])
        ranked_own = sb("ranked_own", [P, E, K])
        rank = sb("rank", [P, K])
        in_slot = sb("in_slot", [P, K, C], BF16)
        base_val = sb("base_val", [P, K, E], BF16)
        k_val = sb("k_val", [P, K, E], BF16)
        empty_far = sb("empty_far", [P, E])
        gather_idx = sb("gather_idx", [P, E], I32)
        scatter_idx = sb("scatter_idx", [P, E], I32)
        cst = sb("cst", [P, DK * D + 2 * DK])
        wt = [sb(f"wt{s}", [P, 2 * DK * F]) for s in range(SLOTS)]
        pair = [sb(f"pair{s}", [P, 2 * D]) for s in range(SLOTS)]
        orow = [sb(f"orow{s}", [P, D]) for s in range(SLOTS)]
        gcur = [sb(f"gcur{s}", [P, 1], I32) for s in range(SLOTS)]
        scur = [sb(f"scur{s}", [P, 1], I32) for s in range(SLOTS)]
        dx = [sb(f"dx{s}", [P, D]) for s in range(2)]
        xT = [sb(f"xT{s}", [P, DK * C]) for s in range(2)]
        xkT = [sb(f"xkT{s}", [P, DK * C]) for s in range(2)]
        xrT = [sb(f"xrT{s}", [P, DK * C]) for s in range(2)]
        relu = sb("relu", [P, 2, HALF])
        hT = sb("hT", [P, 2, HALF])
        gate = [sb(f"gate{s}", [P, D]) for s in range(2)]
        gated = [sb(f"gated{s}", [P, D]) for s in range(2)]

        ps_tr = [psum(f"ps_tr{s}", 2 * DK * C) for s in range(2)]
        ps_h = [psum(f"ps_h{s}", 512) for s in range(2)]
        ps_r = [psum(f"ps_r{s}", 512) for s in range(2)]
        ps_y = [psum(f"ps_y{s}", 512) for s in range(2)]
        ps_base = ps_r[0][:, 0:E]
        ps_list = ps_r[1][:, 0:E]

        w_rT = cst[:, 0:DK * D].rearrange("p (k n) -> p k n", k=DK)
        maa_k = cst[:, DK * D:DK * D + DK]
        maa_r = cst[:, DK * D + DK:DK * D + 2 * DK]

        tok_in = sem("tok_in")
        const_in = sem("const_in")
        out_filled = sem("out_filled")
        tables = sem("tables")
        route = sem("route")
        base_done = sem("base_done")
        slots_ready = sem("slots_ready")
        list_done = sem("list_done")
        w_in = [sem(f"w_in{s}") for s in range(SLOTS)]
        pair_in = [sem(f"pair_in{s}") for s in range(SLOTS)]
        scattered = [sem(f"scattered{s}") for s in range(SLOTS)]
        dx_done = sem("dx_done")
        tr_done = sem("tr_done")
        xT_done = sem("xT_done")
        xk_done = sem("xk_done")
        xr_done = sem("xr_done")
        h_done = sem("h_done")
        relu_done = sem("relu_done")
        sq_done = sem("sq_done")
        r_done = sem("r_done")
        gate_done = sem("gate_done")
        y_done = sem("y_done")
        gated_done = sem("gated_done")
        gcur_done = sem("gcur_done")
        added = sem("added")

        R_COUNTS, R_VALUES, R_LISTS = 5, 6, 12

        def rounds(eng, body):
            for u in range(SLOTS):
                body(u, u)
            with eng.Fori(1, ROUNDS - 1) as i:
                for u in range(SLOTS):
                    body(i * SLOTS + u, u)
            for u in range(SLOTS):
                body((ROUNDS - 1) * SLOTS + u, u)

        def at_least(e, n):
            return e >= n if isinstance(e, int) else True

        def before(e, n):
            return e < n if isinstance(e, int) else True

        block = ctx.enter_context(nc.Block())

        @block.sync
        def _(sp):
            sp.dma_start(tok[:, :], ids.rearrange("(p k) -> p k", k=K)).then_inc(tok_in, 16)
            for e in range(SLOTS):
                sp.dma_start(wt[e][:, :], weights[e]).then_inc(w_in[e], 16)
            with sp.Fori(1, ROUNDS) as i:
                for u in range(SLOTS):
                    sp.wait_ge(y_done, i * SLOTS + (u - SLOTS + 1))
                    sp.dma_start(wt[u][:, :], weights[bass.ds(i * SLOTS + u, 1)].rearrange("a p n -> (a p) n")
                                 ).then_inc(w_in[u], 16)

        @block.gpsimd
        def _(pool):
            pool.iota(etab3[:, :, :], [[pow(HASH_PRIME, -1, E), E], [0, K]], channel_multiplier=0).then_inc(tables, 1)
            pool.memset(not_first[:, :, :], 1.0).then_inc(tables, 1)
            pool.memset(earlier[:, :], 1.0).then_inc(tables, 1)
            pool.wait_ge(tables, 3)
            pool.memset(not_first[:, :, 0:1], 0.0).then_inc(tables, 1)
            pool.affine_select(out=earlier[:, :], in_=earlier[:, :], compare_op=ALU.is_gt, fill=0.0, base=0,
                               pattern=[[1, P]], channel_multiplier=-1).then_inc(tables, 1)
            pool.iota(p_times_k[:, :], [[0, 1]], channel_multiplier=K,
                      allow_small_or_imprecise_dtypes=True).then_inc(tables, 1)
            pool.iota(k_plus1[:, :, :], [[0, E], [1, K]], base=1, channel_multiplier=0,
                      allow_small_or_imprecise_dtypes=True).then_inc(tables, 1)
            pool.iota(slot_no[:, :], [[1, C]], base=1, channel_multiplier=0,
                      allow_small_or_imprecise_dtypes=True).then_inc(tables, 1)
            pool.memset(ident[:, :], 0.0).then_inc(tables, 1)
            pool.wait_ge(tables, 9)
            pool.affine_select(out=ident[:, :], in_=ident[:, :], compare_op=ALU.not_equal, fill=1.0, base=0,
                               pattern=[[-1, P]], channel_multiplier=1).then_inc(tables, 1)

            last_row = pool.to_reg(N - 1)

            def gather(idx, slot):
                pool.indirect_dma_start(pair[slot][:, :], None, pairs,
                                        bass.IndirectOffsetOnAxis(ap=idx.bitcast(U32), axis=0),
                                        bounds_check=last_row, oob_is_err=False).then_inc(pair_in[slot], 16)

            def difference(e, slot, nth):
                pool.wait_ge(pair_in[slot], nth * 16)
                if at_least(e, 2):
                    pool.wait_ge(tr_done, e - 1)
                pool.tensor_tensor(dx[slot % 2][:, :], pair[slot][:, 0:D], pair[slot][:, D:2 * D],
                                   ALU.subtract).then_inc(dx_done, 1)

            pool.wait_ge(route, R_LISTS)
            for e in range(SLOTS):
                gather(gather_idx[:, e:e + 1], e)
            difference(0, 0, 1)
            difference(1, 1, 1)

            def step(e, u):
                i = e // SLOTS if isinstance(e, int) else None
                if before(e, E - 2):
                    nth = ((e + 2) // SLOTS if i is not None else round_of(e, u) + (u + 2) // SLOTS) + 1
                    difference(e + 2, (u + 2) % SLOTS, nth)
                pool.wait_ge(gated_done, e + 1)
                if at_least(e, SLOTS):
                    pool.wait_ge(scattered[u], round_of(e, u) * 16)
                pool.tensor_tensor(orow[u][:, :], pair[u][:, D:2 * D], gated[u % 2][:, :],
                                   ALU.add).then_inc(added, 1)
                pool.wait_ge(out_filled, 16)
                pool.wait_ge(added, e + 1)
                pool.indirect_dma_start(out_rows, bass.IndirectOffsetOnAxis(ap=scur[u][:, :].bitcast(U32), axis=0),
                                        orow[u][:, :], None, bounds_check=last_row,
                                        oob_is_err=False).then_inc(scattered[u], 16)
                if before(e, E - SLOTS):
                    pool.wait_ge(route, R_LISTS)
                    pool.wait_ge(gcur_done, e + 1)
                    gather(gcur[u][:, :], u)

            def round_of(e, u):
                return e // SLOTS if isinstance(e, int) else loop_round[0]

            loop_round = [None]
            for u in range(SLOTS):
                step(u, u)
            with pool.Fori(1, ROUNDS - 1) as i:
                loop_round[0] = i
                for u in range(SLOTS):
                    step(i * SLOTS + u, u)
            for u in range(SLOTS):
                step((ROUNDS - 1) * SLOTS + u, u)
            for u in range(SLOTS):
                pool.wait_ge(scattered[u], ROUNDS * 16)

        @block.scalar
        def _(act):
            act.dma_start(cst[:, :], consts).then_inc(const_in, 16)
            act.dma_start(out.rearrange("b (a t) d -> (b a) (t d)", a=P // B),
                          x.rearrange("b (a t) d -> (b a) (t d)", a=P // B)).then_inc(out_filled, 16)

            def copy_xT(e, par):
                act.wait_ge(tr_done, e + 1)
                nc.scalar.activation(xT[par][:, :], ps_tr[par][:, 0:DK * C], ACT.Copy).then_inc(xT_done, 1)

            def step(e, u):
                for h in range(2):
                    act.wait_ge(h_done, e * 2 + (h + 1))
                    nc.scalar.activation(relu[:, h, :], ps_h[h][:, 0:HALF], ACT.Relu).then_inc(relu_done, 1)
                if before(e, E - 1):
                    copy_xT(e + 1, (u + 1) % 2)
                act.wait_ge(r_done, e + 1)
                nc.scalar.activation(gate[u % 2][:, :], ps_r[u % 2][:, 0:D], ACT.Sigmoid).then_inc(gate_done, 1)

            copy_xT(0, 0)
            rounds(act, step)

        @block.vector
        def _(dve):
            n_route = [0]

            def link(ins):
                n_route[0] += 1
                ins.then_inc(route, 1)

            def linked():
                dve.wait_ge(route, n_route[0])

            dve.wait_ge(tables, 10)
            link(nc.vector.tensor_scalar(etab[:, :, :], etab3[:, :, :], E - 1, None, ALU.bitwise_and))
            dve.wait_ge(tok_in, 16)
            link(nc.vector.tensor_scalar(tok_low[:, :], tok[:, :], E - 1, None, ALU.bitwise_and))
            linked()
            link(nc.vector.tensor_tensor(onehot[:, :, :], etab[:, :, :],
                                         tok_low[:, :].rearrange("p (a k) -> p a k", a=1).broadcast_to([P, E, K]),
                                         ALU.is_equal))
            linked()
            link(nc.vector.tensor_tensor_scan(running[:, :, :].rearrange("p e k -> p (e k)"),
                                              not_first[:, :, :].rearrange("p e k -> p (e k)"),
                                              onehot[:, :, :].rearrange("p e k -> p (e k)"),
                                              0.0, ALU.mult, ALU.add))
            linked()
            link(nc.vector.tensor_copy(counts[:, :], running[:, :, K - 1]))
            nc.vector.tensor_scalar(base_val[:, :, :].rearrange("p k e -> p e k"), onehot[:, :, :],
                                    p_times_k[:, 0:1], None, ALU.mult)
            link(nc.vector.tensor_tensor(k_val[:, :, :].rearrange("p k e -> p e k"), onehot[:, :, :],
                                         k_plus1[:, :, :], ALU.mult))
            dve.wait_ge(base_done, 1)
            link(nc.vector.tensor_tensor(ranked[:, :, :], running[:, :, :],
                                         ps_base.rearrange("p (e a) -> p e a", a=1).broadcast_to([P, E, K]), ALU.add))
            linked()
            link(nc.vector.tensor_tensor(ranked_own[:, :, :], ranked[:, :, :], onehot[:, :, :], ALU.mult))
            linked()
            link(nc.vector.reduce_sum(rank[:, :], ranked_own[:, :, :].rearrange("p e k -> p k e"), AX_X))
            linked()
            for k in range(K):
                nc.vector.tensor_scalar(in_slot[:, k, :], slot_no[:, :], rank[:, k:k + 1], None,
                                        ALU.is_equal).then_inc(slots_ready, 1)
            dve.wait_ge(list_done, 1)
            link(nc.vector.tensor_scalar(gather_idx[:, :], ps_list, -1.0, 0.0, ALU.add, ALU.max))
            link(nc.vector.tensor_scalar(empty_far[:, :], ps_list, 0.0, float(NO_ROW), ALU.is_equal, ALU.mult))
            linked()
            link(nc.vector.scalar_tensor_tensor(scatter_idx[:, :], ps_list, -1.0, empty_far[:, :],
                                                ALU.add, ALU.add))
            assert n_route[0] == R_LISTS, n_route

            dve.wait_ge(const_in, 16)

            def lerp(e, par):
                dve.wait_ge(xT_done, e + 1)
                dxT = ps_tr[par][:, DK * C:2 * DK * C]
                for dst, maa, done in ((xkT, maa_k, xk_done), (xrT, maa_r, xr_done)):
                    for k in range(DK):
                        cols = slice(k * C, (k + 1) * C)
                        ins = nc.vector.scalar_tensor_tensor(dst[par][:, cols], dxT[:, cols], maa[:, k:k + 1],
                                                             xT[par][:, cols], ALU.mult, ALU.add)
                    ins.then_inc(done, 1)

            def close(e, u, i):
                if i is None or not isinstance(i, int) or i > 0:
                    dve.wait_ge(scattered[u], i * 16)
                nc.vector.tensor_copy(scur[u][:, :], scatter_idx[:, bass.ds(e, 1)])
                if before(e, E - SLOTS):
                    nc.vector.tensor_copy(gcur[u][:, :], gather_idx[:, bass.ds(e + SLOTS, 1)]).then_inc(gcur_done, 1)
                dve.wait_ge(gate_done, e + 1)
                if at_least(e, 2):
                    dve.wait_ge(added, e - 1)
                dve.wait_ge(y_done, e + 1)
                nc.vector.tensor_tensor(gated[u % 2][:, :], gate[u % 2][:, :], ps_y[u % 2][:, 0:D],
                                        ALU.mult).then_inc(gated_done, 1)

            def step(e, u, i):
                for h in range(2):
                    dve.wait_ge(relu_done, e * 2 + (h + 1))
                    nc.vector.tensor_tensor(hT[:, h, :], relu[:, h, :], ps_h[h][:, 0:HALF],
                                            ALU.mult).then_inc(sq_done, 1)
                if before(e, E - 1):
                    lerp(e + 1, (u + 1) % 2)
                close(e, u, i)

            lerp(0, 0)
            for u in range(SLOTS):
                step(u, u, 0)
            with dve.Fori(1, ROUNDS - 1) as i:
                for u in range(SLOTS):
                    step(i * SLOTS + u, u, i)
            for u in range(SLOTS):
                step((ROUNDS - 1) * SLOTS + u, u, ROUNDS - 1)

        @block.tensor
        def _(pe):
            pe.wait_ge(tables, 10)
            pe.wait_ge(route, R_COUNTS)
            nc.tensor.matmul(ps_base, earlier[:, :], counts[:, :], start=True, stop=True).then_inc(base_done, 1)
            pe.wait_ge(route, R_VALUES)
            for k in range(K):
                pe.wait_ge(slots_ready, k + 1)
                nc.tensor.matmul(ps_list, in_slot[:, k, :], base_val[:, k, :],
                                 start=(k == 0), stop=False)
                ins = nc.tensor.matmul(ps_list, in_slot[:, k, :], k_val[:, k, :],
                                       start=False, stop=(k == K - 1))
            ins.then_inc(list_done, 1)

            def transpose(e, u):
                pe.wait_ge(dx_done, e + 1)
                for j, src in enumerate((pair[u][:, D:2 * D], dx[u % 2][:, :])):
                    for k in range(DK):
                        c0 = (j * DK + k) * C
                        ins = nc.tensor.transpose(ps_tr[u % 2][:, c0:c0 + C], src[:, k * P:(k + 1) * P], ident[:, :])
                ins.then_inc(tr_done, 1)

            def step(e, u, i):
                w1 = wt[u][:, 0:DK * F].rearrange("p (k f) -> p k f", k=DK)
                w2 = wt[u][:, DK * F:2 * DK * F].rearrange("p (k n) -> p k n", k=FK)
                pe.wait_ge(w_in[u], (i + 1) * 16)
                pe.wait_ge(xk_done, e + 1)
                for f in range(FK):
                    h, c0 = f // 2, f % 2 * C
                    for k in range(DK):
                        ins = nc.tensor.matmul(ps_h[h][:, c0:c0 + C], w1[:, k, f * P:(f + 1) * P],
                                               xkT[u % 2][:, k * C:(k + 1) * C], start=(k == 0), stop=(k == DK - 1))
                    if f % 2 == 1:
                        ins.then_inc(h_done, 1)
                if before(e, E - 1):
                    transpose(e + 1, (u + 1) % SLOTS)
                pe.wait_ge(xr_done, e + 1)
                if at_least(e, 2):
                    pe.wait_ge(gated_done, e - 1)
                for k in range(DK):
                    ins = nc.tensor.matmul(ps_r[u % 2][:, 0:D], xrT[u % 2][:, k * C:(k + 1) * C], w_rT[:, k, :],
                                           start=(k == 0), stop=(k == DK - 1))
                ins.then_inc(r_done, 1)
                for f in range(FK):
                    if f % 2 == 0:
                        pe.wait_ge(sq_done, e * 2 + (f // 2 + 1))
                    c0 = f % 2 * C
                    ins = nc.tensor.matmul(ps_y[u % 2][:, 0:D], hT[:, f // 2, c0:c0 + C], w2[:, f, :],
                                           start=(f == 0), stop=(f == FK - 1))
                ins.then_inc(y_done, 1)

            pe.wait_ge(const_in, 16)
            transpose(0, 0)
            for u in range(SLOTS):
                step(u, u, 0)
            with pe.Fori(1, ROUNDS - 1) as i:
                for u in range(SLOTS):
                    step(i * SLOTS + u, u, i)
            for u in range(SLOTS):
                step((ROUNDS - 1) * SLOTS + u, u, ROUNDS - 1)


def kernel(x, itok_BxS_2_50255, cond_1024, L0_cond_time_maa_k, L0_cond_time_maa_r, L0_cond_w_recept,
           L0_cond_w_key, L0_cond_w_value):
    import numpy as np
    import concourse.bacc as bacc
    from concourse.bass_utils import run_bass_kernel_spmd

    x, cond, ids = np.asarray(x), np.asarray(cond_1024), np.asarray(itok_BxS_2_50255)
    w_r, w_k, w_v = (np.asarray(a) for a in (L0_cond_w_recept, L0_cond_w_key, L0_cond_w_value))
    B, T, D = x.shape
    E, _, F = w_k.shape
    DK, FK = D // P, F // P
    xprev = np.concatenate([cond[:, None, :], x[:, :-1]], axis=1)
    pairs = np.ascontiguousarray(np.concatenate([xprev, x], axis=2).reshape(B * T, 2 * D))
    w1 = w_k.reshape(E, DK, P, F).transpose(0, 2, 1, 3).reshape(E, P, DK * F)
    w2 = w_v.reshape(E, FK, P, D).transpose(0, 2, 1, 3).reshape(E, P, FK * D)
    weights = np.ascontiguousarray(np.concatenate([w1, w2], axis=2))
    w_rT = w_r.T.reshape(DK, P, D).transpose(1, 0, 2).reshape(P, DK * D)
    maa = [np.asarray(a).reshape(DK, P).T for a in (L0_cond_time_maa_k, L0_cond_time_maa_r)]
    consts = np.ascontiguousarray(np.concatenate([w_rT, *maa], axis=1))
    arrays = {"x": np.ascontiguousarray(x), "pairs": pairs, "ids": np.ascontiguousarray(ids.reshape(-1)), "consts": consts, "weights": weights}

    nc = bacc.Bacc("TRN2", target_bir_lowering=False, num_devices=1)
    args = [nc.dram_tensor(n, a.shape, mybir.dt.from_np(a.dtype), kind="ExternalInput").ap()
            for n, a in arrays.items()]
    out = nc.dram_tensor("out", (B, T, D), F32, kind="ExternalOutput").ap()
    build(nc, *args, out)
    r = run_bass_kernel_spmd(nc, [arrays], core_ids=[0])
    return r.results[0]["out"]
```

```python
from contextlib import ExitStack

import concourse.bass as bass
from concourse import mybir

P = 128
HASH_PRIME = 5099

ALU = mybir.AluOpType
ACT = mybir.ActivationFunctionType
AX_X = mybir.AxisListType.X
F32 = mybir.dt.float32
F32R = mybir.dt.float32r
BF16 = mybir.dt.bfloat16
I32 = mybir.dt.int32
U32 = mybir.dt.uint32

SLOTS = 4


def build(nc, x, pairs, ids, consts, weights, out):
    B, T, D = x.shape
    N = B * T
    E = weights.shape[0]
    DK = D // P
    F = weights.shape[2] // (2 * DK)
    FK = F // P
    C = N // E
    K = N // P
    assert C == P and DK == 2 and E == 16 and FK == 4 and K == 16
    NO_ROW = 2 * N
    ROUNDS = E // SLOTS

    out_rows = out.rearrange("b t d -> (b t) d")

    with ExitStack() as ctx:
        def sb(name, shape, dt=F32):
            return ctx.enter_context(nc.sbuf_tensor(name, shape, dt))

        def psum(name, cols):
            return ctx.enter_context(nc.psum_tensor(name, [P, cols], F32))

        def sem(name):
            return ctx.enter_context(nc.semaphore(name))

        POOL_SLOTS, ACT_SLOTS = (4, 8, 13), (5, 10, 15)
        WARM_ROUNDS, WARM = 2, 5
        R_RUNNING, R_VALUES, R_RANK, R_LISTS = 5, 6, 9, 12

        tok = sb("tok", [P, K], I32)
        tok_low = sb("tok_low", [P, K], I32)
        etab3 = sb("etab3", [P, E, K], I32)
        etab = sb("etab", [P, E, K], I32)
        not_first = sb("not_first", [P, E, K], BF16)
        k_plus1 = sb("k_plus1", [P, E, K], BF16)
        p_times_k = sb("p_times_k", [P, 1])
        slot_no = sb("slot_no", [P, C], BF16)
        earlier = sb("earlier", [P, P])
        ident = sb("ident", [P, P])
        onehot = sb("onehot", [P, E, K], BF16)
        running = sb("running", [P, E, K])
        ranked = sb("ranked", [P, E, K])
        ranked_own = sb("ranked_own", [P, E, K])
        rank = sb("rank", [P, K])
        slot_dist = sb("slot_dist", [P, len(ACT_SLOTS), C])
        in_slot = sb("in_slot", [P, K, C], BF16)
        base_val = sb("base_val", [P, K, E], BF16)
        k_val = sb("k_val", [P, K, E], BF16)
        empty_far = sb("empty_far", [P, E])
        gather_idx = sb("gather_idx", [P, E + 2], I32)
        scatter_idx = sb("scatter_idx", [P, E], I32)
        act_warm = sb("act_warm", [P, 1])
        cst = sb("cst", [P, DK * D + 2 * DK])
        wt = [sb(f"wt{s}", [P, 2 * DK * F]) for s in range(SLOTS)]
        pair = [sb(f"pair{s}", [P, 2 * D]) for s in range(SLOTS)]
        resid = [sb(f"resid{s}", [P, D]) for s in range(SLOTS)]
        orow = [sb(f"orow{s}", [P, D]) for s in range(SLOTS)]
        gcur = [sb(f"gcur{s}", [P, 1], I32) for s in range(SLOTS)]
        scur = [sb(f"scur{s}", [P, 1], I32) for s in range(SLOTS)]
        dx = [sb(f"dx{s}", [P, D]) for s in range(2)]
        xT = [sb(f"xT{s}", [P, DK * C]) for s in range(2)]
        xkT = [sb(f"xkT{s}", [P, DK * C]) for s in range(2)]
        xrT = [sb(f"xrT{s}", [P, DK * C]) for s in range(2)]
        relu = sb("relu", [P, FK * C])
        hT = sb("hT", [P, FK * C])
        w_rT_hi, w_rT_lo = (sb(f"w_rT_{x}", [P, DK * D], F32R) for x in ("hi", "lo"))
        xrT_hi, xrT_lo = ([sb(f"xrT_{x}{s}", [P, DK * C], F32R) for s in range(2)] for x in ("hi", "lo"))
        w2_hi, w2_lo = ([sb(f"w2_{x}{s}", [P, FK * D], F32R) for s in range(2)] for x in ("hi", "lo"))
        hT_hi, hT_lo = ([sb(f"hT_{x}{s}", [P, FK * C], F32R) for s in range(2)] for x in ("hi", "lo"))
        gate = [sb(f"gate{s}", [P, D]) for s in range(2)]
        gated = [sb(f"gated{s}", [P, D]) for s in range(2)]

        ps_tr = [psum(f"ps_tr{s}", 2 * DK * C) for s in range(2)]
        ps_h = [psum(f"ps_h{s}", 512) for s in range(2)]
        ps_r = [psum(f"ps_r{s}", 512) for s in range(2)]
        ps_y = [psum(f"ps_y{s}", 512) for s in range(2)]
        ps_base = ps_r[0][:, 0:E]
        ps_list = ps_r[1][:, 0:E]

        w_rT = cst[:, 0:DK * D]
        maa_k = cst[:, DK * D:DK * D + DK]
        maa_r = cst[:, DK * D + DK:DK * D + 2 * DK]

        tok_in = sem("tok_in")
        const_in = sem("const_in")
        out_filled = sem("out_filled")
        act_warm_set = sem("act_warm_set")
        tables = sem("tables")
        route = sem("route")
        base_done = sem("base_done")
        slots_ready = sem("slots_ready")
        pool_slots_ready = sem("pool_slots_ready")
        act_slots_ready = sem("act_slots_ready")
        slot_dist_done = sem("slot_dist_done")
        list_done = sem("list_done")
        w_in = [sem(f"w_in{s}") for s in range(SLOTS)]
        pair_in = [sem(f"pair_in{s}") for s in range(SLOTS)]
        scattered = [sem(f"scattered{s}") for s in range(SLOTS)]
        dx_done = sem("dx_done")
        tr_done = sem("tr_done")
        xT_done = sem("xT_done")
        xk_done = sem("xk_done")
        xr_done = sem("xr_done")
        h_done = sem("h_done")
        relu_done = sem("relu_done")
        sq_done = sem("sq_done")
        hT_hi_done = sem("hT_hi_done")
        hT_lo_done = sem("hT_lo_done")
        w_rT_hi_done = sem("w_rT_hi_done")
        w_rT_lo_done = sem("w_rT_lo_done")
        xr_hi_done = sem("xr_hi_done")
        xr_lo_done = sem("xr_lo_done")
        w2_hi_done = sem("w2_hi_done")
        w2_lo_done = sem("w2_lo_done")
        r_done = sem("r_done")
        gate_done = sem("gate_done")
        y_done = sem("y_done")
        gated_done = sem("gated_done")
        gcur_done = sem("gcur_done")
        added = sem("added")
        last_added = sem("last_added")
        resid_done = sem("resid_done")

        def rounds(eng, body):
            for u in range(SLOTS):
                body(u, u)
            with eng.Fori(1, ROUNDS - 1) as i:
                loop_round[0] = i
                for u in range(SLOTS):
                    body(i * SLOTS + u, u)
            for u in range(SLOTS):
                body((ROUNDS - 1) * SLOTS + u, u)

        loop_round = [None]

        def round_of(e):
            return e // SLOTS if isinstance(e, int) else loop_round[0]

        def at_least(e, n):
            return e >= n if isinstance(e, int) else True

        def before(e, n):
            return e < n if isinstance(e, int) else True

        def fill(eng, batches):
            for b in batches:
                eng.dma_start(out[b].rearrange("(a t) d -> a (t d)", a=32),
                              x[b].rearrange("(a t) d -> a (t d)", a=32)).then_inc(out_filled, 16)

        block = ctx.enter_context(nc.Block())

        @block.sync
        def _(sp):
            sp.dma_start(tok[:, :], ids.rearrange("(p k) -> p k", k=K)).then_inc(tok_in, 16)
            for e in range(SLOTS):
                if e == 2:
                    sp.wait_ge(pair_in[0], 16)
                sp.dma_start(wt[e][:, :], weights[e]).then_inc(w_in[e], 16)
            fill(sp, range(1, B))
            with sp.Fori(1, ROUNDS) as i:
                for u in range(SLOTS):
                    sp.wait_ge(hT_lo_done, i * SLOTS + (u - SLOTS + 1))
                    sp.dma_start(wt[u][:, :], weights[bass.ds(i * SLOTS + u, 1)].rearrange("a p n -> (a p) n")
                                 ).then_inc(w_in[u], 16)

        @block.gpsimd
        def _(pool):
            pool.iota(etab3[:, :, :], [[pow(HASH_PRIME, -1, E), E], [0, K]], channel_multiplier=0).then_inc(tables, 1)
            pool.memset(not_first[:, :, :], 1.0).then_inc(tables, 1)
            pool.memset(earlier[:, :], 1.0).then_inc(tables, 1)
            pool.wait_ge(tables, 3)
            pool.memset(not_first[:, :, 0:1], 0.0).then_inc(tables, 1)
            pool.affine_select(out=earlier[:, :], in_=earlier[:, :], compare_op=ALU.is_gt, fill=0.0, base=0,
                               pattern=[[1, P]], channel_multiplier=-1).then_inc(tables, 1)
            pool.iota(p_times_k[:, :], [[0, 1]], channel_multiplier=K,
                      allow_small_or_imprecise_dtypes=True).then_inc(tables, 1)
            pool.iota(k_plus1[:, :, :], [[0, E], [1, K]], base=1, channel_multiplier=0,
                      allow_small_or_imprecise_dtypes=True).then_inc(tables, 1)
            pool.iota(slot_no[:, :], [[1, C]], base=1, channel_multiplier=0,
                      allow_small_or_imprecise_dtypes=True).then_inc(tables, 1)
            pool.memset(ident[:, :], 0.0).then_inc(tables, 1)
            pool.wait_ge(tables, 9)
            pool.affine_select(out=ident[:, :], in_=ident[:, :], compare_op=ALU.not_equal, fill=1.0, base=0,
                               pattern=[[-1, P]], channel_multiplier=1).then_inc(tables, 1)

            pool.wait_ge(route, R_RANK)
            for k in POOL_SLOTS:
                pool.tensor_scalar(in_slot[:, k, :], slot_no[:, :], rank[:, k:k + 1], None,
                                   ALU.is_equal).then_inc(pool_slots_ready, 1)

            last_row = pool.to_reg(N - 1)

            def gather(idx, slot):
                pool.indirect_dma_start(pair[slot][:, :], None, pairs,
                                        bass.IndirectOffsetOnAxis(ap=idx.bitcast(U32), axis=0),
                                        bounds_check=last_row, oob_is_err=False).then_inc(pair_in[slot], 16)

            def difference(e, slot, nth):
                pool.wait_ge(pair_in[slot], nth * 16)
                pool.wait_ge(tr_done, e - 1)
                pool.tensor_tensor(dx[slot % 2][:, :], pair[slot][:, 0:D], pair[slot][:, D:2 * D],
                                   ALU.subtract).then_inc(dx_done, 1)

            pool.wait_ge(route, R_LISTS)
            for e in range(SLOTS):
                gather(gather_idx[:, e:e + 1], e)
            pool.wait_ge(resid_done, 1)
            pool.wait_ge(gcur_done, 1)
            gather(gcur[0][:, :], 0)

            def step(e, u):
                if before(e, E - SLOTS):
                    pool.wait_ge(resid_done, e + 2)
                if before(e, E - 3):
                    difference(e + 3, (u + 3) % SLOTS, round_of(e) + (u + 3) // SLOTS + 1)
                if before(e, E - SLOTS):
                    pool.wait_ge(route, R_LISTS)
                    pool.wait_ge(gcur_done, e + 2)
                    gather(gcur[(u + 1) % SLOTS][:, :], (u + 1) % SLOTS)
                if before(e, E - 1):
                    pool.wait_ge(gated_done, e + 1)
                    if at_least(e, SLOTS):
                        pool.wait_ge(scattered[u], round_of(e) * 16)
                    pool.tensor_tensor(orow[u][:, :], resid[u][:, :], gated[u % 2][:, :],
                                       ALU.add).then_inc(added, 1)
                pool.wait_ge(out_filled, 16 * B)
                if before(e, E - 1):
                    pool.wait_ge(added, e + 1)
                else:
                    pool.wait_ge(last_added, 1)
                pool.indirect_dma_start(out_rows, bass.IndirectOffsetOnAxis(ap=scur[u][:, :].bitcast(U32), axis=0),
                                        orow[u][:, :], None, bounds_check=last_row,
                                        oob_is_err=False).then_inc(scattered[u], 16)

            rounds(pool, step)
            for u in range(SLOTS):
                pool.wait_ge(scattered[u], ROUNDS * 16)

        @block.scalar
        def _(act):
            act.dma_start(cst[:, :], consts).then_inc(const_in, 16)
            fill(act, range(1))
            act.wait_ge(act_warm_set, 1)
            nc.scalar.activation(act_warm[:, :], act_warm[:, :], ACT.Sigmoid)

            def copy_xT(e, par):
                act.wait_ge(tr_done, e + 1)
                nc.scalar.activation(xT[par][:, :], ps_tr[par][:, 0:DK * C], ACT.Copy).then_inc(xT_done, 1)

            def round_xr(e, par):
                act.wait_ge(xr_done, e + 1)
                nc.scalar.activation(xrT_hi[par][:, :], xrT[par][:, :], ACT.Copy).then_inc(xr_hi_done, 1)

            def round_w2(e, u, nth):
                act.wait_ge(w_in[u], nth * 16)
                if at_least(e, 2):
                    act.wait_ge(y_done, e - 1)
                nc.scalar.activation(w2_hi[u % 2][:, :], wt[u][:, DK * F:2 * DK * F],
                                     ACT.Copy).then_inc(w2_hi_done, 1)

            def step(e, u):
                par, ahead = u % 2, (u + 1) % 2
                act.wait_ge(h_done, e + 1)
                nc.scalar.activation(relu[:, :], ps_h[par][:, 0:FK * C], ACT.Relu).then_inc(relu_done, 1)
                if at_least(e, 1) and before(e, E - 1):
                    copy_xT(e + 1, ahead)
                act.wait_ge(relu_done, e + 1)
                if at_least(e, 1):
                    act.wait_ge(hT_lo_done, e)
                nc.scalar.activation(hT[:, :], relu[:, :], ACT.Square).then_inc(sq_done, 1)
                act.wait_ge(sq_done, e + 1)
                if at_least(e, 2):
                    act.wait_ge(y_done, e - 1)
                nc.scalar.activation(hT_hi[par][:, :], hT[:, :], ACT.Copy).then_inc(hT_hi_done, 1)
                if before(e, E - 1):
                    round_xr(e + 1, ahead)
                    if at_least(e, 1):
                        round_w2(e + 1, (u + 1) % SLOTS, round_of(e) + (u + 1) // SLOTS + 1)
                act.wait_ge(r_done, e + 1)
                nc.scalar.activation(gate[par][:, :], ps_r[par][:, 0:D], ACT.Sigmoid).then_inc(gate_done, 1)

            act.wait_ge(const_in, 16)
            nc.scalar.activation(w_rT_hi[:, :], w_rT, ACT.Copy).then_inc(w_rT_hi_done, 1)
            act.wait_ge(route, R_RANK)
            for n, k in enumerate(ACT_SLOTS):
                nc.scalar.activation(slot_dist[:, n, :], slot_no[:, :], ACT.Square, bias=rank[:, k:k + 1],
                                     scale=-1.0).then_inc(slot_dist_done, 1)
                act.wait_ge(slot_dist_done, n + 1)
                nc.scalar.activation(in_slot[:, k, :], slot_dist[:, n, :], ACT.Relu, bias=1.0,
                                     scale=-1.0).then_inc(act_slots_ready, 1)
            for e in range(2):
                round_w2(e, e, 1)
            copy_xT(0, 0)
            copy_xT(1, 1)
            round_xr(0, 0)
            rounds(act, step)

        @block.vector
        def _(dve):
            n_route = [0]

            def link(ins):
                n_route[0] += 1
                ins.then_inc(route, 1)

            def linked():
                dve.wait_ge(route, n_route[0])

            link(nc.vector.memset(gather_idx[:, E:E + 2], NO_ROW))
            nc.vector.memset(act_warm[:, :], 0.0).then_inc(act_warm_set, 1)
            dve.wait_ge(tables, 1)
            link(nc.vector.tensor_scalar(etab[:, :, :], etab3[:, :, :], E - 1, None, ALU.bitwise_and))
            dve.wait_ge(tok_in, 16)
            link(nc.vector.tensor_scalar(tok_low[:, :], tok[:, :], E - 1, None, ALU.bitwise_and))
            linked()
            link(nc.vector.tensor_tensor(onehot[:, :, :], etab[:, :, :],
                                         tok_low[:, :].rearrange("p (a k) -> p a k", a=1).broadcast_to([P, E, K]),
                                         ALU.is_equal))
            linked()
            dve.wait_ge(tables, 10)
            link(nc.vector.tensor_tensor_scan(running[:, :, :].rearrange("p e k -> p (e k)"),
                                              not_first[:, :, :].rearrange("p e k -> p (e k)"),
                                              onehot[:, :, :].rearrange("p e k -> p (e k)"),
                                              0.0, ALU.mult, ALU.add))
            linked()
            nc.vector.tensor_scalar(base_val[:, :, :].rearrange("p k e -> p e k"), onehot[:, :, :],
                                    p_times_k[:, 0:1], None, ALU.mult)
            link(nc.vector.tensor_tensor(k_val[:, :, :].rearrange("p k e -> p e k"), onehot[:, :, :],
                                         k_plus1[:, :, :], ALU.mult))
            dve.wait_ge(base_done, 1)
            link(nc.vector.tensor_tensor(ranked[:, :, :], running[:, :, :],
                                         ps_base.rearrange("p (e a) -> p e a", a=1).broadcast_to([P, E, K]), ALU.add))
            linked()
            link(nc.vector.tensor_tensor(ranked_own[:, :, :], ranked[:, :, :], onehot[:, :, :], ALU.mult))
            linked()
            link(nc.vector.reduce_sum(rank[:, :], ranked_own[:, :, :].rearrange("p e k -> p k e"), AX_X))
            linked()
            for k in range(K):
                if k not in POOL_SLOTS + ACT_SLOTS:
                    nc.vector.tensor_scalar(in_slot[:, k, :], slot_no[:, :], rank[:, k:k + 1], None,
                                            ALU.is_equal).then_inc(slots_ready, 1)
            dve.wait_ge(list_done, 1)
            link(nc.vector.tensor_scalar(gather_idx[:, 0:E], ps_list, -1.0, 0.0, ALU.add, ALU.max))
            link(nc.vector.tensor_scalar(empty_far[:, :], ps_list, 0.0, float(NO_ROW), ALU.is_equal, ALU.mult))
            linked()
            link(nc.vector.scalar_tensor_tensor(scatter_idx[:, :], ps_list, -1.0, empty_far[:, :],
                                                ALU.add, ALU.add))
            assert n_route[0] == R_LISTS, n_route

            def lerp(par, dst, maa, done):
                dxT = ps_tr[par][:, DK * C:2 * DK * C]
                for k in range(DK):
                    cols = slice(k * C, (k + 1) * C)
                    ins = nc.vector.scalar_tensor_tensor(dst[par][:, cols], dxT[:, cols], maa[:, k:k + 1],
                                                         xT[par][:, cols], ALU.mult, ALU.add)
                ins.then_inc(done, 1)

            def rest(dst, whole, hi, done):
                nc.vector.tensor_tensor(dst, whole, hi.bitcast(F32), ALU.subtract).then_inc(done, 1)

            def rest_xr(e, par):
                dve.wait_ge(xr_hi_done, e + 1)
                rest(xrT_lo[par][:, :], xrT[par][:, :], xrT_hi[par][:, :], xr_lo_done)

            def rest_h(e, par):
                dve.wait_ge(hT_hi_done, e + 1)
                rest(hT_lo[par][:, :], hT[:, :], hT_hi[par][:, :], hT_lo_done)

            def rest_w2(e, u):
                dve.wait_ge(w2_hi_done, e + 1)
                rest(w2_lo[u % 2][:, :], wt[u][:, DK * F:2 * DK * F], w2_hi[u % 2][:, :], w2_lo_done)

            def first_difference(e):
                dve.wait_ge(pair_in[e], 16)
                if e == 2:
                    dve.wait_ge(tr_done, 1)
                nc.vector.tensor_tensor(dx[e % 2][:, :], pair[e][:, 0:D], pair[e][:, D:2 * D],
                                        ALU.subtract).then_inc(dx_done, 1)

            def lerp_k(e, u):
                dve.wait_ge(xT_done, e + 1)
                lerp(u % 2, xkT, maa_k, xk_done)

            def lerp_r(e, u):
                lerp(u % 2, xrT, maa_r, xr_done)
                nc.vector.tensor_copy(resid[u][:, :], pair[u][:, D:2 * D]).then_inc(resid_done, 1)

            def lerps(e, u):
                lerp_k(e, u)
                lerp_r(e, u)

            def next_list(e, u):
                nc.vector.tensor_copy(gcur[u][:, :], gather_idx[:, bass.ds(e, 1)]).then_inc(gcur_done, 1)

            def close(e, u, i):
                if not (isinstance(i, int) and i == 0):
                    dve.wait_ge(scattered[u], i * 16)
                nc.vector.tensor_copy(scur[u][:, :], scatter_idx[:, bass.ds(e, 1)])
                if before(e, E - SLOTS):
                    next_list(e + SLOTS + 2, (u + 2) % SLOTS)
                if at_least(e, 2):
                    dve.wait_ge(added, e - 1)
                dve.wait_ge(gate_done, e + 1)
                dve.wait_ge(y_done, e + 1)
                nc.vector.tensor_tensor(gated[u % 2][:, :], gate[u % 2][:, :], ps_y[u % 2][:, 0:D],
                                        ALU.mult).then_inc(gated_done, 1)

            def last_residual():
                u = (E - 1) % SLOTS
                dve.wait_ge(gated_done, E)
                dve.wait_ge(scattered[u], (ROUNDS - 1) * 16)
                nc.vector.tensor_tensor(orow[u][:, :], resid[u][:, :], gated[u % 2][:, :],
                                        ALU.add).then_inc(last_added, 1)

            def step(e, u):
                close(e, u, round_of(e))
                if before(e, E - 1):
                    rest_h(e + 1, (u + 1) % 2)
                if before(e, E - 2):
                    rest_xr(e + 2, u % 2)
                if before(e, E - 3):
                    lerps(e + 3, (u + 3) % SLOTS)
                if before(e, E - 2):
                    rest_w2(e + 2, (u + 2) % SLOTS)

            dve.wait_ge(const_in, 16)
            dve.wait_ge(w_rT_hi_done, 1)
            rest(w_rT_lo[:, :], w_rT, w_rT_hi[:, :], w_rT_lo_done)
            rest_w2(0, 0)
            for ahead in range(2):
                next_list(SLOTS + ahead, ahead)
            first_difference(0)
            first_difference(1)
            lerps(0, 0)
            lerp_k(1, 1)
            rest_xr(0, 0)
            first_difference(2)
            lerp_r(1, 1)
            rest_h(0, 0)
            rest_xr(1, 1)
            lerps(2, 2)
            rest_w2(1, 1)
            rounds(dve, step)
            last_residual()

        @block.tensor
        def _(pe):
            pe.wait_ge(tables, 10)
            pe.wait_ge(route, R_RUNNING)
            nc.tensor.matmul(ps_base, earlier[:, :], running[:, :, K - 1], start=True, stop=True).then_inc(base_done, 1)
            pe.wait_ge(route, R_VALUES)
            for k in range(K):
                n_pool, n_act = (sum(j <= k for j in share) for share in (POOL_SLOTS, ACT_SLOTS))
                if k in POOL_SLOTS:
                    pe.wait_ge(pool_slots_ready, n_pool)
                elif k in ACT_SLOTS:
                    pe.wait_ge(act_slots_ready, n_act)
                else:
                    pe.wait_ge(slots_ready, k + 1 - n_pool - n_act)
                nc.tensor.matmul(ps_list, in_slot[:, k, :], base_val[:, k, :],
                                 start=(k == 0), stop=False)
                ins = nc.tensor.matmul(ps_list, in_slot[:, k, :], k_val[:, k, :],
                                       start=False, stop=(k == K - 1))
            ins.then_inc(list_done, 1)

            def transpose(e, u):
                pe.wait_ge(dx_done, e + 1)
                for j, src in enumerate((pair[u][:, D:2 * D], dx[u % 2][:, :])):
                    for k in range(DK):
                        c0 = (j * DK + k) * C
                        ins = nc.tensor.transpose(ps_tr[u % 2][:, c0:c0 + C], src[:, k * P:(k + 1) * P], ident[:, :])
                ins.then_inc(tr_done, 1)

            def first_product(e, u, nth):
                w1 = wt[u][:, 0:DK * F].rearrange("p (k f) -> p k f", k=DK)
                pe.wait_ge(w_in[u], nth * 16)
                pe.wait_ge(xk_done, e + 1)
                for f in range(FK):
                    for k in range(DK):
                        ins = nc.tensor.matmul(ps_h[u % 2][:, f * C:(f + 1) * C], w1[:, k, f * P:(f + 1) * P],
                                               xkT[u % 2][:, k * C:(k + 1) * C], start=(k == 0), stop=(k == DK - 1))
                ins.then_inc(h_done, 1)


            def receptance(e, par):
                if at_least(e, 2):
                    pe.wait_ge(gated_done, e - 1)
                parts = ((xrT_hi, w_rT_hi), (xrT_hi, w_rT_lo), (xrT_lo, w_rT_hi))
                for n, (a, b) in enumerate(parts):
                    if n == 0:
                        pe.wait_ge(xr_hi_done, e + 1)
                    if n == 2:
                        pe.wait_ge(xr_lo_done, e + 1)
                    for k in range(DK):
                        ins = nc.tensor.matmul(ps_r[par][:, 0:D], a[par][:, k * C:(k + 1) * C],
                                               b[:, k * D:(k + 1) * D], start=(n == k == 0),
                                               stop=(n == 2 and k == DK - 1))
                ins.then_inc(r_done, 1)

            def second_product(e, par):
                if at_least(e, 2):
                    pe.wait_ge(gated_done, e - 1)
                parts = ((hT_hi, w2_hi, hT_hi_done), (hT_hi, w2_lo, w2_lo_done), (hT_lo, w2_hi, hT_lo_done))
                for n, (a, b, ready) in enumerate(parts):
                    if n == 0:
                        pe.wait_ge(w2_hi_done, e + 1)
                    pe.wait_ge(ready, e + 1)
                    for f in range(FK):
                        ins = nc.tensor.matmul(ps_y[par][:, 0:D], a[par][:, f * C:(f + 1) * C],
                                               b[par][:, f * D:(f + 1) * D], start=(n == f == 0),
                                               stop=(n == 2 and f == FK - 1))
                ins.then_inc(y_done, 1)

            def step(e, u):
                second_product(e, u % 2)
                if before(e, E - 1):
                    receptance(e + 1, (u + 1) % 2)
                if before(e, E - 2):
                    first_product(e + 2, (u + 2) % SLOTS, round_of(e) + (u + 2) // SLOTS + 1)
                if before(e, E - 3):
                    transpose(e + 3, (u + 3) % SLOTS)

            def keep_warm(n):
                for _ in range(n):
                    nc.tensor.matmul(ps_y[1][:, :], in_slot[:, 0, :], in_slot[:, 0:4, :], start=True, stop=True)

            with pe.Fori(0, WARM_ROUNDS):
                keep_warm(WARM)
            transpose(0, 0)
            keep_warm(2)
            transpose(1, 1)
            first_product(0, 0, 1)
            first_product(1, 1, 1)
            pe.wait_ge(w_rT_hi_done, 1)
            pe.wait_ge(w_rT_lo_done, 1)
            receptance(0, 0)
            transpose(2, 2)
            rounds(pe, step)


def kernel(x, itok_BxS_2_50255, cond_1024, L0_cond_time_maa_k, L0_cond_time_maa_r, L0_cond_w_recept,
           L0_cond_w_key, L0_cond_w_value):
    import numpy as np
    import concourse.bacc as bacc
    from concourse.bass_utils import run_bass_kernel_spmd

    x, cond, ids = np.asarray(x), np.asarray(cond_1024), np.asarray(itok_BxS_2_50255)
    w_r, w_k, w_v = (np.asarray(a) for a in (L0_cond_w_recept, L0_cond_w_key, L0_cond_w_value))
    B, T, D = x.shape
    E, _, F = w_k.shape
    DK, FK = D // P, F // P
    xprev = np.concatenate([cond[:, None, :], x[:, :-1]], axis=1)
    pairs = np.ascontiguousarray(np.concatenate([xprev, x], axis=2).reshape(B * T, 2 * D))
    w1 = w_k.reshape(E, DK, P, F).transpose(0, 2, 1, 3).reshape(E, P, DK * F)
    w2 = w_v.reshape(E, FK, P, D).transpose(0, 2, 1, 3).reshape(E, P, FK * D)
    weights = np.ascontiguousarray(np.concatenate([w1, w2], axis=2))
    w_rT = w_r.T.reshape(DK, P, D).transpose(1, 0, 2).reshape(P, DK * D)
    maa = [np.asarray(a).reshape(DK, P).T for a in (L0_cond_time_maa_k, L0_cond_time_maa_r)]
    consts = np.ascontiguousarray(np.concatenate([w_rT, *maa], axis=1))
    arrays = {"x": np.ascontiguousarray(x), "pairs": pairs, "ids": np.ascontiguousarray(ids.reshape(-1)), "consts": consts, "weights": weights}

    nc = bacc.Bacc("TRN2", target_bir_lowering=False, num_devices=1)
    args = [nc.dram_tensor(n, a.shape, mybir.dt.from_np(a.dtype), kind="ExternalInput").ap()
            for n, a in arrays.items()]
    out = nc.dram_tensor("out", (B, T, D), F32, kind="ExternalOutput").ap()
    build(nc, *args, out)
    r = run_bass_kernel_spmd(nc, [arrays], core_ids=[0])
    return r.results[0]["out"]
```
